# Optimizing a Trainium2 kernel written in Bass

```python
import numpy as np
import jax
import jax.numpy as jnp

def _softmax(x, axis=-1):
    return jax.nn.softmax(x, axis=axis)

def _gelu(x):
    return jax.nn.gelu(x, approximate=True)

def _silu(x):
    return jax.nn.silu(x)

def _sigmoid(x):
    return jax.nn.sigmoid(x)

def _layernorm(x, axis=-1, eps=1e-05):
    m = jnp.mean(x, axis=axis, keepdims=True)
    v = jnp.var(x, axis=axis, keepdims=True)
    return (x - m) / jnp.sqrt(v + eps)

def _scatter_add(tgt, idx, src, axis=0):
    return tgt.at[idx].add(src)

def _segment_sum(src, seg, n):
    return jax.ops.segment_sum(src, seg, n)
kernel_name = 'mk_gnn_resnorm_d1_gnn_r32_eec80a'

def setup_inputs(seed: int=0):
    np.random.seed(seed)
    _w = jnp.asarray

    def _rec_inputs():
        import jax
        import jax.numpy as jnp
        _gk = jax.random.key(seed)
        x = -0.0001126 + 1 * jax.random.normal(jax.random.fold_in(_gk, 1), (50000, 768), jnp.float32)
        src = jax.random.randint(jax.random.fold_in(_gk, 2), (25000,), 0, 50000, jnp.int32)
        dst = jax.random.randint(jax.random.fold_in(_gk, 3), (25000,), 0, 50000, jnp.int32)
        _o = jnp.argsort(dst, stable=True)
        src = src[_o]
        dst = dst[_o]
        return (x, src, dst)
    x, src, dst = _rec_inputs()

    def _L0_gnn_setup():
        import jax, jax.numpy as jnp
        import numpy as np
        N_NODES = 10000
        N_EDGES = 3125
        DIM = 768
        key = jax.random.key(seed)
        k1, k2, k3, k4 = jax.random.split(key, 4)
        x = jax.random.normal(k1, (N_NODES, DIM), dtype=jnp.float32)
        edge_index = jax.random.randint(k2, (2, N_EDGES), 0, N_NODES, dtype=jnp.int32)
        W = jax.random.normal(k3, (DIM, DIM), dtype=jnp.float32) / np.sqrt(DIM)
        b = jnp.zeros((DIM,), dtype=jnp.float32)
        return {'x': x, 'edge_index': edge_index, 'W': W, 'b': b}
    _L0_gnn_all = _L0_gnn_setup()
    _L0_gnn_in = {k: v for k, v in _L0_gnn_all.items() if k in ('W', 'b')}
    del _L0_gnn_all
    return {'x': x, 'src': src, 'dst': dst, 'L0_gnn_W': _L0_gnn_in['W'], 'L0_gnn_b': _L0_gnn_in['b']}

def reference(x, src, dst, L0_gnn_W, L0_gnn_b):
    import jax
    import jax.numpy as jnp

    def _L0_gnn_ref(x, edge_index, W, b):
        import jax, jax.numpy as jnp
        import numpy as np
        N_NODES = 10000
        N_EDGES = 3125
        DIM = 768
        n = x.shape[0]
        loop = jnp.arange(n, dtype=edge_index.dtype)
        src = jnp.concatenate([edge_index[0], loop])
        dst = jnp.concatenate([edge_index[1], loop])
        deg = jax.ops.segment_sum(jnp.ones_like(dst, dtype=x.dtype), dst, num_segments=n)
        deg_inv_sqrt = jnp.where(deg > 0, jax.lax.rsqrt(deg), 0.0)
        norm = deg_inv_sqrt[src] * deg_inv_sqrt[dst]
        h = x @ W
        msg = h[src] * norm[:, None]
        out = jax.ops.segment_sum(msg, dst, num_segments=n)
        return out + b
    edge_index = jnp.stack([src, dst])
    x = _layernorm(x + _L0_gnn_ref(x, edge_index, L0_gnn_W, L0_gnn_b), axis=-1)
    return x

_drawn_inputs = setup_inputs


def setup_inputs(seed=0):
    import zlib

    import numpy as np

    out = dict(_drawn_inputs(seed))
    spreads = {'L0_gnn_b': (0.0, 0.1)}
    factors = {}
    for name, (base, spread) in spreads.items():
        noise = np.random.default_rng([zlib.crc32(name.encode()), seed]).standard_normal(out[name].shape)
        drawn = base * np.exp(spread * noise) if base else spread * noise
        out[name] = jnp.asarray(drawn.astype(out[name].dtype))
    for name, factor in factors.items():
        out[name] = (out[name] * factor).astype(out[name].dtype)
    return out
```

```python
from contextlib import ExitStack

import concourse.bass as bass
from concourse import mybir

ALU = mybir.AluOpType
ACT = mybir.ActivationFunctionType
AX = mybir.AxisListType
F32 = mybir.dt.float32
F32R = mybir.dt.float32r
BF16 = mybir.dt.bfloat16
F16 = mybir.dt.float16
I32 = mybir.dt.int32

P = 128
EPS = 1e-5
S_FALL, S_COUNTS, S_INVERSE, S_DINV = 8, 9, 11, 15
CONSTS = 11
C_TICKS = 6
UNROLL = 6
HEAD = 6
FAR = 1 << 16


class Tile:

    def __init__(self, i, off):
        self.i, self.off = i, off

    def __add__(self, d):
        return Tile(self.i, self.off + d)

    def __sub__(self, d):
        return Tile(self.i, self.off - d)

    @property
    def n(self):
        return self.i * UNROLL + self.off

    def slot(self, ring):
        return self.off % ring

    def round(self, ring):
        return self.i * (UNROLL // ring) + self.off // ring


def at_least(eng, sem, value):
    if not isinstance(value, int) or value > 0:
        eng.wait_ge(sem, value)


def gnn_kernel(nc, x, edges, w, b, out):
    NODES, D = x.shape
    EDGES = edges.shape[0]
    KC = D // P
    HALF = D // 2
    TILES = -(-NODES // P)
    LAST_ROWS = NODES - (TILES - 1) * P
    TCOLS = -(-TILES // 8) * 8
    TBLK = TCOLS // 4
    EP = max(p for p in range(1, P + 1) if EDGES % p == 0)
    EC = EDGES // EP
    ROUNDS = (TILES - HEAD - 6) // UNROLL
    LOOP_END = HEAD + ROUNDS * UNROLL
    HIST_UNROLL = 4
    assert D % P == 0 and HALF <= 512 and EC % HIST_UNROLL == 0 and TBLK <= P and TCOLS <= 512

    source_weight = nc.dram_tensor("source_weight", (TCOLS * P, 1), F32, kind="Internal").ap()
    edge_list = nc.dram_tensor("edge_list", (TCOLS * P, 2), I32, kind="Internal").ap()
    node_sums = nc.dram_tensor("node_sums", ((TCOLS + 1) * P, D), F32, kind="Internal").ap()

    with ExitStack() as ctx:
        def sb(name, shape, dt):
            return ctx.enter_context(nc.sbuf_tensor(name, shape, dt))

        def pb(name, shape, dt=F32):
            return ctx.enter_context(nc.psum_tensor(name, shape, dt))

        def sem(name):
            return ctx.enter_context(nc.semaphore(name))

        w_raw = sb("w_raw", [P, KC, D], F32)
        w_hi = sb("w_hi", [P, KC, D], F32R)
        w_lo = sb("w_lo", [P, KC, D], F32R)
        bias = sb("bias", [P, D], F32)
        eps = sb("eps", [P, 1], F32)
        iota_i = sb("iota_i", [P, TCOLS], I32)
        pid_i = sb("pid_i", [P, 1], I32)
        tile_i = sb("tile_i", [P, TCOLS], I32)
        iota_h = sb("iota_h", [P, TCOLS], F16)
        iota_f = sb("iota_f", [P, P], F32)
        centred = sb("centred", [P, P], F32)
        centre = sb("centre", [P, TCOLS], F32)
        pid_f = sb("pid_f", [P, 1], F32)
        ident = sb("ident", [P, P], F32)
        ones = sb("ones", [P, TCOLS], F32)
        zeros = sb("zeros", [P, D], F32)
        zeros_h = sb("zeros_h", [P, TCOLS], BF16)
        edge_sb = sb("edge_sb", [EP, EC, 2], I32)
        next_edge = sb("next_edge", [EP, 2], I32)
        dst_hi_i = sb("dst_hi_i", [EP, EC], I32)
        dst_lo_i = sb("dst_lo_i", [EP, EC], I32)
        dst_hi = sb("dst_hi", [EP, EC], F32)
        dst_lo = sb("dst_lo", [EP, EC], F32)
        hot_hi = sb("hot_hi", [EP, HIST_UNROLL, TCOLS], BF16)
        hot_lo = sb("hot_lo", [EP, HIST_UNROLL, P], BF16)
        falls = sb("falls", [EP, EC], F32)
        fall = sb("fall", [EP, 1], F32)
        degree = sb("degree", [P, TCOLS], F32)
        count_sb = sb("count_sb", [P, TCOLS], F32)
        inverse = sb("inverse", [P, TCOLS], F32)
        guess = sb("guess", [P, TCOLS], F32)
        newton = sb("newton", [P, TCOLS], F32)
        dinv = sb("dinv", [P, TCOLS], F32)
        dinv_rows = sb("dinv_rows", [TBLK, 4, P], F32)
        tile_edges = sb("tile_edges", [1, TCOLS], F32)
        running = sb("running", [1, TCOLS], F32)
        before = sb("before", [1, TCOLS], F32)
        start_row = sb("start_row", [1, TCOLS], I32)
        most = sb("most", [1, 2], F32)
        general_f = sb("general_f", [1, 1], F32)
        general = sb("general", [1, 1], I32)
        XR, WR, GR, OR = 6, 6, 3, 3
        x_t = sb("x_t", [P, XR, D], F32)
        window = sb("window", [P, WR, 2], I32)
        rel = sb("rel", [P, WR], F32)
        square = sb("square", [P, WR], F32)
        outside = sb("outside", [P, WR], F32)
        index = sb("index", [P, WR], I32)
        g_t = sb("g_t", [P, GR, D], F32)
        g_w = sb("g_w", [P, GR], F32)
        xs_t = sb("xs_t", [P, 2, D], F32)
        gh_t = sb("gh_t", [P, 2, D], F32R)
        gl_t = sb("gl_t", [P, 2, D], F32R)
        s_t = sb("s_t", [P, 2, P], F32R)
        zh_t = sb("zh_t", [P, 2, KC, P], F32R)
        zl_t = sb("zl_t", [P, 2, KC, P], F32R)
        y_t = sb("y_t", [P, 2, D], F32)
        stats = sb("stats", [P, 2, 2, 6], F32)
        moments = sb("moments", [P, 2, 2], F32)
        std = sb("std", [P, 2], F32)
        rstd = sb("rstd", [P, 2], F32)
        shift = sb("shift", [P, 2], F32)
        o_t = sb("o_t", [P, OR, D], F32)
        c_src = sb("c_src", [EP, 1], I32)
        c_dst = sb("c_dst", [EP, 1], F32)
        c_to = sb("c_to", [EP, 1], I32)
        c_row = sb("c_row", [EP, 1], F32)
        c_shift = sb("c_shift", [EP, 1], F32)
        c_spare = sb("c_spare", [EP, 1], F32)
        c_weight = sb("c_weight", [EP, 1], F32)
        c_rows_t = sb("c_rows_t", [EP, D], F32)
        c_sum = sb("c_sum", [EP, D], F32)
        c_spread_t = sb("c_spread_t", [EP, P], F32)
        c_same_t = sb("c_same_t", [EP, EP], F32)
        c_earlier = sb("c_earlier", [EP, EP], F32)
        c_below = sb("c_below", [EP, EP], F32)
        own_pair = sb("own_pair", [P, TCOLS, 2], I32)
        z_ps = [pb(f"z_ps{k}", [P, 2, 512]) for k in range(2)]
        o_ps = [pb(f"o_ps{k}", [P, 2, 512]) for k in range(2)]

        def z_flat(k):
            return z_ps[k][:, :, :].rearrange("p a b -> p (a b)")[:, 0:D]

        hist_ps = z_ps[0][:, 0, 0:TCOLS]
        count_ps = z_ps[0][0:1, 1, 0:TCOLS]
        fall_ps = z_ps[1][0:1, 0, 0:1]
        dinv_ps = o_ps[0][0:TBLK, 0, :]

        w_in, b_in, edges_in, next_in = sem("w_in"), sem("b_in"), sem("edges_in"), sem("next_in")
        iotas, consts = sem("iotas"), sem("consts")
        set_up = sem("set_up")
        hot_ready, hot_used, hist_ready = sem("hot_ready"), sem("hot_used"), sem("hist_ready")
        counts_ready, guess_ready, dinv_ready = sem("counts_ready"), sem("guess_ready"), sem("dinv_ready")
        dinv_turned, dinv_copied = sem("dinv_turned"), sem("dinv_copied")
        weights_out, list_out = sem("weights_out"), sem("list_out")
        starts_ready, general_ready = sem("starts_ready"), sem("general_ready")
        w_hi_ready, w_split = sem("w_hi_ready"), sem("w_split")
        ring_zeroed = sem("ring_zeroed")
        x_in = [sem(f"x_in{k}") for k in range(XR)]
        window_in = [sem(f"window_in{k}") for k in range(WR)]
        g_in = [sem(f"g_in{k}") for k in range(GR)]
        o_out = [sem(f"o_out{k}") for k in range(OR)]
        rel_ready, square_ready, outside_ready, index_ready = sem("rel_ready"), sem("square_ready"), sem("outside_ready"), sem("index_ready")
        xs_ready, gh_ready, gl_ready, s_ready = sem("xs_ready"), sem("gh_ready"), sem("gl_ready"), sem("s_ready")
        z_ready, zh_ready, zl_ready = sem("z_ready"), sem("zh_ready"), sem("zl_ready")
        product_ready, y_ready, yb_ready = sem("product_ready"), sem("y_ready"), sem("yb_ready")
        stats_ready, moments_ready, std_ready = sem("stats_ready"), sem("moments_ready"), sem("std_ready")
        rstd_ready, shift_ready, o_ready = sem("rstd_ready"), sem("shift_ready"), sem("o_ready")
        paced = sem("paced")
        c_rows, c_cur, c_spread, c_turned, c_same = (sem(f"c_{s}") for s in ("rows", "cur", "spread", "turned", "same"))
        c_scaled, c_index, c_summed, c_new, c_out = (sem(f"c_{s}") for s in ("scaled", "index", "summed", "new", "out"))
        c_vec, c_init, own_ready = sem("c_vec"), sem("c_init"), sem("own_ready")
        sums_zeroed, general_done, ones_out = sem("sums_zeroed"), sem("general_done"), sem("ones_out")

        block = ctx.enter_context(nc.Block())

        @block.sync
        def _(sp):
            def load_x(t, rows=P):
                at_least(sp, y_ready, (t - XR).n + 1)
                sp.dma_start(x_t[0:rows, t.slot(XR), :], x[bass.ds(t.n * P, rows), :]
                             ).then_inc(x_in[t.slot(XR)], 16)

            def load_window(t):
                at_least(sp, index_ready, (t - WR).round(3) + 1)
                start = sp.value_load(start_row[0:1, bass.ds(t.n, 1)], min_val=0, max_val=(TCOLS - 1) * P)
                sp.dma_start(window[:, t.slot(WR), :], edge_list[bass.ds(start, P), :]
                             ).then_inc(window_in[t.slot(WR)], 16)

            sp.dma_start(edge_sb[:, :, :], edges.rearrange("(p c) k -> p c k", p=EP)).then_inc(edges_in, 16)
            sp.wait_ge(consts, 1)
            sp.dma_start(next_edge[0:EP - 1, :], edges.rearrange("(p c) k -> p c k", p=EP)[1:EP, 0, :]
                         ).then_inc(next_in, 16)
            sp.dma_start(edge_list[0:EDGES, :], edges).then_inc(list_out, 16)
            sp.dma_start(w_raw[:, :, :], w.rearrange("(c p) n -> p c n", p=P)).then_inc(w_in, 16)
            sp.dma_start(bias[:, :], b.partition_broadcast(P)).then_inc(b_in, 16)
            for k in range(XR):
                load_x(Tile(0, k))
            sp.wait_ge(dinv_copied, 1)
            sp.dma_start(source_weight.rearrange("(k t p) o -> t k (p o)", k=4, p=P), dinv_rows[:, :, :]
                         ).then_inc(weights_out, 16)
            sp.wait_ge(list_out, 16)
            sp.wait_ge(general_ready, 1)
            taken = sp.value_load(general[0:1, 0:1], min_val=0, max_val=1)
            with sp.If(taken > 0):
                with sp.Fori(0, TCOLS + 1) as r:
                    sp.dma_start(node_sums[bass.ds(r * P, P), :], zeros[:, :]).then_inc(sums_zeroed, 16)
                sp.wait_ge(general_done, 1)
            sp.wait_ge(starts_ready, 1)
            for k in range(2 * WR):
                load_window(Tile(0, k))
            with sp.Fori(0, (TILES - 2 * XR) // UNROLL) as i:
                for k in range(XR):
                    load_x(Tile(i, XR + k))
                    load_window(Tile(i, XR + k) + WR)
            done = XR + (TILES - 2 * XR) // UNROLL * UNROLL
            for k in range(done, TILES):
                load_x(Tile(0, k), P if k < TILES - 1 else LAST_ROWS)
                if k + WR < TILES:
                    load_window(Tile(0, k) + WR)

        @block.gpsimd
        def _(pool):
            pool.iota(iota_i[:, :], [[1, TCOLS]], base=0, channel_multiplier=0).then_inc(iotas, 1)
            pool.iota(tile_i[:, :], [[P, TCOLS]], base=0, channel_multiplier=0).then_inc(iotas, 1)
            pool.iota(pid_i[:, :], [[0, 1]], base=0, channel_multiplier=1).then_inc(iotas, 1)
            pool.memset(g_t[:, :, :], 0.0).then_inc(ring_zeroed, 1)
            pool.memset(g_w[:, :], 0.0).then_inc(ring_zeroed, 1)
            pool.wait_ge(ring_zeroed, 2)
            pool.wait_ge(weights_out, 16)
            pool.wait_ge(general_ready, 1)

            def gather(t, rows):
                at_least(pool, index_ready, t.round(3) + 1)
                pool.sem_inc(paced, 1)
                at_least(pool, gl_ready, (t - GR).n + 1)
                pool.sem_inc(paced, 1)
                at = index[:, t.slot(WR):t.slot(WR) + 1]
                pool.indirect_dma_start(out=g_t[:, t.slot(GR), :], out_offset=None, in_=rows,
                                        in_offset=bass.IndirectOffsetOnAxis(ap=at, axis=0),
                                        bounds_check=NODES - 1, oob_is_err=False
                                        ).then_inc(g_in[t.slot(GR)], 16)
                pool.indirect_dma_start(out=g_w[:, t.slot(GR):t.slot(GR) + 1], out_offset=None, in_=source_weight,
                                        in_offset=bass.IndirectOffsetOnAxis(ap=at, axis=0),
                                        bounds_check=NODES - 1, oob_is_err=False
                                        ).then_inc(g_in[t.slot(GR)], 16)

            def gather_all(rows):
                for k in range(HEAD):
                    gather(Tile(0, k), rows)
                with pool.Fori(0, ROUNDS) as i:
                    for k in range(UNROLL):
                        gather(Tile(i, HEAD + k), rows)
                for k in range(LOOP_END, TILES):
                    gather(Tile(0, k), rows)

            def chunk(c):
                pool.wait_ge(c_index, c + 1)
                pool.sem_inc(paced, 1)
                pool.indirect_dma_start(out=c_rows_t[:, :], out_offset=None, in_=x,
                                        in_offset=bass.IndirectOffsetOnAxis(ap=c_src[:, :], axis=0)
                                        ).then_inc(c_rows, 16)
                pool.indirect_dma_start(out=c_weight[:, :], out_offset=None, in_=source_weight,
                                        in_offset=bass.IndirectOffsetOnAxis(ap=c_src[:, :], axis=0)
                                        ).then_inc(c_rows, 16)
                pool.indirect_dma_start(out=c_sum[:, :], out_offset=None, in_=node_sums,
                                        in_offset=bass.IndirectOffsetOnAxis(ap=c_to[:, :], axis=0)
                                        ).then_inc(c_cur, 16)
                pool.wait_ge(c_new, (c + 1) * 2)
                pool.sem_inc(paced, 1)
                pool.indirect_dma_start(out=node_sums, out_offset=bass.IndirectOffsetOnAxis(ap=c_to[:, :], axis=0),
                                        in_=c_sum[:, :], in_offset=None).then_inc(c_out, 16)
                pool.wait_ge(c_out, (c + 1) * 16)

            taken = pool.value_load(general[0:1, 0:1], min_val=0, max_val=1)
            with pool.If(taken > 0):
                pool.wait_ge(sums_zeroed, 16 * (TCOLS + 1))
                with pool.Fori(0, EC) as c:
                    chunk(c)
                pool.iota(own_pair[:, :, :], [[1, TCOLS], [0, 2]], base=0, channel_multiplier=TCOLS
                          ).then_inc(own_ready, 1)
                pool.wait_ge(own_ready, 1)
                pool.dma_start(source_weight.rearrange("(p t) o -> p (t o)", p=P), ones[:, :]).then_inc(ones_out, 16)
                pool.dma_start(edge_list.rearrange("(p t) k -> p (t k)", p=P),
                               own_pair[:, :, :].rearrange("p t k -> p (t k)")).then_inc(ones_out, 16)
                pool.wait_ge(ones_out, 32)
                pool.sem_inc(general_done, 1)
                gather_all(node_sums)
            with pool.Else():
                gather_all(x)

        @block.scalar
        def _(act):
            act.wait_ge(w_in, 16)
            nc.scalar.copy(w_hi[:, :, :], w_raw[:, :, :]).then_inc(w_hi_ready, 1)
            act.wait_ge(set_up, S_INVERSE)
            nc.scalar.activation(guess[:, :], inverse[:, :], ACT.Sqrt).then_inc(guess_ready, 1)

            def scale_x(t):
                act.wait_ge(x_in[t.slot(XR)], 16 * (t.round(XR) + 1))
                at_least(act, z_ready, (t - 2).n + 1)
                nc.scalar.activation(xs_t[:, t.slot(2), :], x_t[:, t.slot(XR), :], ACT.Copy,
                                     scale=dinv[:, bass.ds(t.n, 1)]).then_inc(xs_ready, 1)

            def gathered_high(t):
                act.wait_ge(g_in[t.slot(GR)], 32 * (t.round(GR) + 1))
                at_least(act, z_ready, (t - 2).n + 1)
                nc.scalar.activation(gh_t[:, t.slot(2), :], g_t[:, t.slot(GR), :], ACT.Copy,
                                     scale=g_w[:, t.slot(GR):t.slot(GR) + 1]).then_inc(gh_ready, 1)

            def z_high(t):
                act.wait_ge(z_ready, t.n + 1)
                at_least(act, product_ready, (t - 2).n + 1)
                nc.scalar.copy(zh_t[:, t.slot(2), :, :].rearrange("p c n -> p (c n)"),
                               z_flat(t.slot(2))).then_inc(zh_ready, 1)

            def root(t):
                act.wait_ge(moments_ready, t.n + 1)
                k = t.slot(2)
                nc.scalar.activation(std[:, k:k + 1], moments[:, k, 1:2], ACT.Sqrt, bias=eps[:, :]
                                     ).then_inc(std_ready, 1)

            def normalise(t):
                act.wait_ge(shift_ready, t.n + 1)
                at_least(act, o_out[t.slot(OR)], 16 * t.round(OR))
                k = t.slot(2)
                nc.scalar.activation(o_t[:, t.slot(OR), :], y_t[:, k, :], ACT.Identity, scale=rstd[:, k:k + 1],
                                     bias=shift[:, k:k + 1]).then_inc(o_ready, 1)

            def store(t, rows=P):
                act.wait_ge(o_ready, t.n + 1)
                act.dma_start(out[bass.ds(t.n * P, rows), :], o_t[0:rows, t.slot(OR), :]
                              ).then_inc(o_out[t.slot(OR)], 16)

            def step(t, last=False):
                if not (isinstance(t.i, int) and t.off >= TILES):
                    z_high(t)
                if not (isinstance(t.i, int) and t.off < 3):
                    normalise(t - 3)
                if not (isinstance(t.i, int) and t.off + 2 >= TILES):
                    scale_x(t + 2)
                    gathered_high(t + 2)
                if not (isinstance(t.i, int) and t.off < 3):
                    store(t - 3)
                if not (isinstance(t.i, int) and not 2 <= t.off < TILES + 2):
                    root(t - 2)

            act.wait_ge(set_up, S_DINV)
            for k in range(2):
                scale_x(Tile(0, k))
                gathered_high(Tile(0, k))
            for k in range(HEAD):
                step(Tile(0, k))
            with act.Fori(0, ROUNDS) as i:
                for k in range(UNROLL):
                    step(Tile(i, HEAD + k))
            for k in range(LOOP_END, TILES + 2):
                step(Tile(0, k))
            normalise(Tile(0, TILES - 1))
            store(Tile(0, TILES - 1), LAST_ROWS)
            for k in range(OR):
                act.wait_ge(o_out[k], 16 * len(range(k, TILES, OR)))

        @block.vector
        def _(dve):
            steps = [0]

            def after(ins):
                ins.then_inc(set_up, 1)
                steps[0] += 1
                return steps[0]

            dve.memset(next_edge[:, :], 1 << 24).then_inc(consts, 1)
            dve.memset(ones[:, :], 1.0).then_inc(consts, 1)
            dve.memset(zeros[:, :], 0.0).then_inc(consts, 1)
            dve.memset(zeros_h[:, :], 0.0).then_inc(consts, 1)
            dve.memset(eps[:, :], EPS).then_inc(consts, 1)
            dve.wait_ge(iotas, 3)
            dve.tensor_copy(iota_h[:, :], iota_i[:, :]).then_inc(consts, 1)
            dve.tensor_copy(iota_f[:, :], iota_i[:, 0:P]).then_inc(consts, 1)
            dve.tensor_scalar(centred[:, :], iota_i[:, 0:P], 63.5, None, ALU.subtract).then_inc(consts, 1)
            dve.tensor_scalar(centre[:, :], tile_i[:, :], 63.5, None, ALU.add).then_inc(consts, 1)
            dve.tensor_copy(pid_f[:, :], pid_i[:, :]).then_inc(consts, 1)
            dve.wait_ge(consts, CONSTS - 1)
            dve.tensor_scalar(ident[:, :], iota_f[:, :], pid_f[:, 0:1], None, ALU.is_equal).then_inc(consts, 1)

            dve.wait_ge(edges_in, 16)
            after(dve.tensor_scalar(dst_hi_i[:, :], edge_sb[:, :, 1], 7, None, ALU.logical_shift_right))
            a = after(dve.tensor_scalar(dst_lo_i[:, :], edge_sb[:, :, 1], P - 1, None, ALU.bitwise_and))
            dve.wait_ge(set_up, a)
            after(dve.tensor_copy(dst_hi[:, :], dst_hi_i[:, :]))
            a = after(dve.tensor_copy(dst_lo[:, :], dst_lo_i[:, :]))
            dve.wait_ge(set_up, a)

            def one_hot(c, k):
                dve.tensor_scalar(hot_hi[:, k, :], iota_h[0:EP, :], dst_hi[:, bass.ds(c, 1)], None,
                                  ALU.is_equal).then_inc(hot_ready, 1)
                dve.tensor_scalar(hot_lo[:, k, :], iota_h[0:EP, 0:P], dst_lo[:, bass.ds(c, 1)], None,
                                  ALU.is_equal).then_inc(hot_ready, 1)

            for k in range(HIST_UNROLL):
                one_hot(k, k)
            with dve.Fori(0, EC // HIST_UNROLL - 1) as i:
                for k in range(HIST_UNROLL):
                    dve.wait_ge(hot_used, i * HIST_UNROLL + k + 1)
                    one_hot(i * HIST_UNROLL + HIST_UNROLL + k, k)

            dve.wait_ge(next_in, 16)
            after(dve.tensor_tensor(falls[:, 0:EC - 1], edge_sb[:, 0:EC - 1, 1], edge_sb[:, 1:EC, 1], ALU.subtract))
            a = after(dve.tensor_tensor(falls[:, EC - 1:EC], edge_sb[:, EC - 1, 1:2], next_edge[:, 1:2], ALU.subtract))
            dve.wait_ge(set_up, a)
            a = after(dve.tensor_reduce(fall[:, :], falls[:, :], AX.X, ALU.max))
            dve.wait_ge(set_up, a)
            a = after(dve.tensor_scalar(fall[:, :], fall[:, :], 0.0, None, ALU.is_gt))
            assert a == S_FALL

            dve.wait_ge(hist_ready, 1)
            a = after(dve.tensor_copy(count_sb[:, :], hist_ps))
            assert a == S_COUNTS
            dve.wait_ge(set_up, a)
            a = after(dve.tensor_scalar(degree[:, :], count_sb[:, :], 1.0, None, ALU.add))
            dve.wait_ge(set_up, a)
            a = after(dve.reciprocal(inverse[:, :], degree[:, :]))
            assert a == S_INVERSE
            dve.wait_ge(guess_ready, 1)
            a = after(dve.tensor_tensor(newton[:, :], guess[:, :], guess[:, :], ALU.mult))
            dve.wait_ge(set_up, a)
            a = after(dve.tensor_tensor(newton[:, :], newton[:, :], degree[:, :], ALU.mult))
            dve.wait_ge(set_up, a)
            a = after(dve.tensor_scalar(newton[:, :], newton[:, :], -0.5, 1.5, ALU.mult, ALU.add))
            dve.wait_ge(set_up, a)
            a = after(dve.tensor_tensor(dinv[:, :], newton[:, :], guess[:, :], ALU.mult))
            assert a == S_DINV
            dve.wait_ge(dinv_turned, 1)
            dve.tensor_copy(dinv_rows[:, :, :], dinv_ps.rearrange("t (k p) -> t k p", k=4)).then_inc(dinv_copied, 1)

            dve.wait_ge(counts_ready, 1)
            a = after(dve.tensor_copy(tile_edges[:, :], count_ps))
            dve.wait_ge(set_up, a)
            after(dve.tensor_reduce(most[:, 0:1], tile_edges[:, :], AX.X, ALU.max))
            a = after(dve.tensor_tensor_scan(running[:, :], tile_edges[:, :], zeros[0:1, 0:TCOLS], 0.0,
                                             ALU.add, ALU.add))
            dve.wait_ge(set_up, a)
            after(dve.tensor_tensor(before[:, :], running[:, :], tile_edges[:, :], ALU.subtract))
            a = after(dve.tensor_scalar(most[:, 1:2], most[:, 0:1], float(P), None, ALU.is_gt))
            dve.wait_ge(set_up, a)
            a = after(dve.tensor_tensor(general_f[:, :], most[:, 1:2], fall_ps, ALU.add))
            dve.wait_ge(set_up, a)
            dve.tensor_scalar(general[:, :], general_f[:, :], 0.0, None, ALU.is_gt).then_inc(general_ready, 1)
            dve.wait_ge(w_hi_ready, 1)
            dve.tensor_tensor(w_lo[:, :, :], w_raw[:, :, :], w_hi[:, :, :].bitcast(F32), ALU.subtract).then_inc(w_split, 1)
            dve.wait_ge(general_ready, 1)

            def chunk(c):
                tick = [0]

                def then(ins):
                    ins.then_inc(c_vec, 1)
                    tick[0] += 1
                    dve.wait_ge(c_vec, c * C_TICKS + tick[0])

                dve.tensor_copy(c_src[:, :], edge_sb[:, bass.ds(c, 1), 0]).then_inc(c_vec, 1)
                tick[0] += 1
                then(dve.tensor_copy(c_dst[:, :], edge_sb[:, bass.ds(c, 1), 1]))
                dve.tensor_scalar(c_spread_t[:, :], ones[0:EP, 0:P], c_dst[:, 0:1], None, ALU.mult
                                  ).then_inc(c_spread, 1)
                dve.wait_ge(c_turned, c + 1)
                dve.tensor_scalar(c_same_t[:, :], o_ps[1][0:EP, 0, 0:EP], c_dst[:, 0:1], None, ALU.is_equal
                                  ).then_inc(c_same, 1)
                dve.wait_ge(c_same, c + 1)
                then(dve.tensor_tensor(c_earlier[:, :], c_same_t[:, :], c_below[:, :], ALU.mult))
                then(dve.tensor_reduce(c_spare[:, :], c_earlier[:, :], AX.X, ALU.max))
                then(dve.tensor_tensor(c_shift[:, :], c_row[:, :], c_dst[:, :], ALU.subtract))
                then(dve.tensor_tensor(c_shift[:, :], c_shift[:, :], c_spare[:, :], ALU.mult))
                dve.tensor_tensor(c_to[:, :], c_shift[:, :], c_dst[:, :], ALU.add).then_inc(c_index, 1)
                dve.wait_ge(c_rows, (c + 1) * 32)
                dve.tensor_scalar(c_rows_t[:, :], c_rows_t[:, :], c_weight[:, 0:1], None, ALU.mult
                                  ).then_inc(c_scaled, 1)
                dve.wait_ge(c_summed, c + 1)
                dve.wait_ge(c_cur, (c + 1) * 16)
                for h in range(2):
                    part = c_sum[:, h * HALF:(h + 1) * HALF]
                    dve.tensor_tensor(part, part, o_ps[0][0:EP, h, 0:HALF], ALU.add).then_inc(c_new, 1)
                dve.wait_ge(c_out, (c + 1) * 16)
                assert tick[0] == C_TICKS

            taken = dve.value_load(general[0:1, 0:1], min_val=0, max_val=1)
            with dve.If(taken > 0):
                dve.tensor_scalar(c_below[:, :], iota_f[0:EP, 0:EP], pid_f[0:EP, 0:1], None, ALU.is_lt
                                  ).then_inc(c_init, 1)
                dve.tensor_scalar(c_row[:, :], pid_f[0:EP, :], float(TCOLS * P), None, ALU.add).then_inc(c_init, 1)
                dve.wait_ge(c_init, 2)
                with dve.Fori(0, EC) as c:
                    chunk(c)
                dve.tensor_copy(start_row[:, :], tile_i[0:1, :]).then_inc(starts_ready, 1)
            with dve.Else():
                dve.tensor_scalar(start_row[:, :], before[:, :], float(EDGES - P), None, ALU.min
                                  ).then_inc(starts_ready, 1)

            def make_index(t):
                n = 3 if not isinstance(t.i, int) else min(3, TILES - t.off)
                for k in range(n):
                    u = t + k
                    dve.wait_ge(window_in[u.slot(WR)], 16 * (u.round(WR) + 1))
                a, z = t.slot(WR), t.slot(WR) + n
                done = t.round(3)
                at_least(dve, s_ready, (t - 4).n + 1)
                dve.tensor_tensor(rel[:, a:z], window[:, a:z, 1], centre[:, bass.ds(t.n, n)], ALU.subtract
                                  ).then_inc(rel_ready, 1)
                dve.wait_ge(rel_ready, done + 1)
                dve.tensor_tensor(square[:, a:z], rel[:, a:z], rel[:, a:z], ALU.mult).then_inc(square_ready, 1)
                dve.wait_ge(square_ready, done + 1)
                dve.tensor_scalar(outside[:, a:z], square[:, a:z], 64.0 ** 2, float(FAR), ALU.is_gt, ALU.mult
                                  ).then_inc(outside_ready, 1)
                dve.wait_ge(outside_ready, done + 1)
                dve.tensor_tensor(index[:, a:z], outside[:, a:z], window[:, a:z, 0], ALU.add
                                  ).then_inc(index_ready, 1)

            def gathered_low(t):
                k, g = t.slot(2), t.slot(GR)
                at_least(dve, z_ready, (t - 2).n + 1)
                dve.wait_ge(gh_ready, t.n + 1)
                dve.scalar_tensor_tensor(out=gl_t[:, k, :], in0=g_t[:, g, :], scalar=g_w[:, g:g + 1],
                                         in1=gh_t[:, k, :].bitcast(F32), op0=ALU.mult, op1=ALU.subtract
                                         ).then_inc(gl_ready, 1)

            def select(t):
                at_least(dve, z_ready, (t - 2).n + 1)
                dve.tensor_scalar(s_t[:, t.slot(2), :], centred[:, :], rel[:, t.slot(WR):t.slot(WR) + 1], None,
                                  ALU.is_equal).then_inc(s_ready, 1)

            def z_low(t):
                k = t.slot(2)
                dve.wait_ge(zh_ready, t.n + 1)
                dve.tensor_tensor(zl_t[:, k, :, :].rearrange("p c n -> p (c n)"), z_flat(k),
                                  zh_t[:, k, :, :].rearrange("p c n -> p (c n)").bitcast(F32), ALU.subtract
                                  ).then_inc(zl_ready, 1)

            def add_up(t):
                k = t.slot(2)
                dve.wait_ge(product_ready, t.n + 1)
                at_least(dve, o_ready, (t - 2).n + 1)
                dve.scalar_tensor_tensor(out=y_t[:, k, :].rearrange("p (h n) -> p h n", h=2),
                                         in0=o_ps[k][:, :, 0:HALF], scalar=dinv[:, bass.ds(t.n, 1)],
                                         in1=x_t[:, t.slot(XR), :].rearrange("p (h n) -> p h n", h=2),
                                         op0=ALU.mult, op1=ALU.add).then_inc(y_ready, 1)
                dve.wait_ge(y_ready, t.n + 1)
                dve.tensor_tensor(y_t[:, k, :], y_t[:, k, :], bias[:, :], ALU.add).then_inc(yb_ready, 1)

            def measure(t, between):
                k = t.slot(2)
                dve.wait_ge(yb_ready, t.n + 1)
                for h in range(2):
                    dve.bn_stats(stats[:, k, h, :], y_t[:, k, h * HALF:(h + 1) * HALF]).then_inc(stats_ready, 1)
                dve.wait_ge(stats_ready, t.n * 2 + 2)
                if between:
                    select(between)
                dve.bn_aggr(moments[:, k, :], stats[:, k, :, :].rearrange("p h s -> p (h s)")
                            ).then_inc(moments_ready, 1)

            def finish(t):
                k = t.slot(2)
                dve.wait_ge(std_ready, t.n + 1)
                dve.reciprocal(rstd[:, k:k + 1], std[:, k:k + 1]).then_inc(rstd_ready, 1)
                dve.wait_ge(rstd_ready, t.n + 1)
                dve.scalar_tensor_tensor(out=shift[:, k:k + 1], in0=moments[:, k, 0:1], scalar=-1.0,
                                         in1=rstd[:, k:k + 1], op0=ALU.mult, op1=ALU.mult).then_inc(shift_ready, 1)

            def step(t):
                peeled = isinstance(t.i, int)
                if not (peeled and t.off >= TILES):
                    z_low(t)
                if not (peeled and t.off < 3):
                    finish(t - 3)
                if not (peeled and not 2 <= t.off < TILES + 2):
                    add_up(t - 2)
                if not (peeled and t.off + 2 >= TILES):
                    gathered_low(t + 2)
                following = None if peeled and t.off + 2 >= TILES else t + 2
                if not (peeled and not 2 <= t.off < TILES + 2):
                    measure(t - 2, following)
                elif following:
                    select(following)
                if t.off % 3 == 0 and not (peeled and t.off + 6 >= TILES):
                    make_index(t + 6)

            dve.wait_ge(b_in, 16)
            make_index(Tile(0, 0))
            make_index(Tile(0, 3))
            for k in range(2):
                gathered_low(Tile(0, k))
                select(Tile(0, k))
            for k in range(HEAD):
                step(Tile(0, k))
            with dve.Fori(0, ROUNDS) as i:
                for k in range(UNROLL):
                    step(Tile(i, HEAD + k))
            for k in range(LOOP_END, TILES + 2):
                step(Tile(0, k))
            finish(Tile(0, TILES - 1))

        @block.tensor
        def _(pe):
            pe.wait_ge(consts, CONSTS)
            nc.tensor.matmul(hist_ps, zeros_h[:, 0:P], zeros_h[:, :], start=True, stop=False)
            with pe.Fori(0, EC // HIST_UNROLL) as i:
                for k in range(HIST_UNROLL):
                    pe.wait_ge(hot_ready, (i * HIST_UNROLL + k) * 2 + 2)
                    nc.tensor.matmul(hist_ps, hot_lo[:, k, :], hot_hi[:, k, :], start=False, stop=False
                                     ).then_inc(hot_used, 1)
            nc.tensor.matmul(hist_ps, zeros_h[:, 0:P], zeros_h[:, :], start=False, stop=True).then_inc(hist_ready, 1)
            pe.wait_ge(set_up, S_COUNTS)
            nc.tensor.matmul(fall_ps, fall[:, :], ones[0:EP, 0:1], start=True, stop=True)
            nc.tensor.matmul(count_ps, ones[:, 0:1], count_sb[:, :], start=True, stop=True).then_inc(counts_ready, 1)
            pe.wait_ge(set_up, S_DINV)
            for k in range(4):
                ins = nc.tensor.transpose(dinv_ps[:, k * P:(k + 1) * P], dinv[:, k * TBLK:(k + 1) * TBLK], ident[:, :])
            ins.then_inc(dinv_turned, 1)

            pe.wait_ge(general_ready, 1)
            taken = pe.value_load(general[0:1, 0:1], min_val=0, max_val=1)
            with pe.If(taken > 0):
                pe.wait_ge(dinv_copied, 1)
                with pe.Fori(0, EC) as c:
                    pe.wait_ge(c_spread, c + 1)
                    nc.tensor.transpose(o_ps[1][:, 0, 0:EP], c_spread_t[:, :], ident[0:EP, 0:EP]).then_inc(c_turned, 1)
                    pe.wait_ge(c_scaled, c + 1)
                    for h in range(2):
                        ins = nc.tensor.matmul(o_ps[0][0:EP, h, 0:HALF], c_same_t[:, :],
                                               c_rows_t[:, h * HALF:(h + 1) * HALF], start=True, stop=True)
                    ins.then_inc(c_summed, 1)

            def sum_rows(t):
                k = t.slot(2)
                pe.wait_ge(xs_ready, t.n + 1)
                pe.wait_ge(s_ready, t.n + 1)
                pe.wait_ge(gl_ready, t.n + 1)
                at_least(pe, zl_ready, (t - 2).n + 1)
                for c in range(KC):
                    cols = slice(c * P, (c + 1) * P)
                    z = z_flat(k)[:, cols]
                    nc.tensor.matmul(z, xs_t[:, k, cols], ident[:, :], is_transpose=True, start=True, stop=False)
                    nc.tensor.matmul(z, gh_t[:, k, cols], s_t[:, k, :], start=False, stop=False)
                    ins = nc.tensor.matmul(z, gl_t[:, k, cols], s_t[:, k, :], start=False, stop=True)
                ins.then_inc(z_ready, 1)

            def multiply(t):
                k = t.slot(2)
                pe.wait_ge(zh_ready, t.n + 1)
                at_least(pe, y_ready, (t - 2).n + 1)
                for c in range(KC):
                    for part in (w_hi, w_lo):
                        for h in range(2):
                            nc.tensor.matmul(o_ps[k][:, h, 0:HALF], zh_t[:, k, c, :],
                                             part[:, c, h * HALF:(h + 1) * HALF],
                                             start=(c == 0 and part is w_hi), stop=False)
                pe.wait_ge(zl_ready, t.n + 1)
                for c in range(KC):
                    for h in range(2):
                        ins = nc.tensor.matmul(o_ps[k][:, h, 0:HALF], zl_t[:, k, c, :],
                                               w_hi[:, c, h * HALF:(h + 1) * HALF], start=False, stop=(c == KC - 1))
                ins.then_inc(product_ready, 1)

            pe.wait_ge(dinv_copied, 1)
            pe.wait_ge(w_split, 1)
            for k in range(HEAD):
                sum_rows(Tile(0, k))
                if k:
                    multiply(Tile(0, k - 1))
            with pe.Fori(0, ROUNDS) as i:
                for k in range(UNROLL):
                    sum_rows(Tile(i, HEAD + k))
                    multiply(Tile(i, HEAD + k - 1))
            for k in range(LOOP_END, TILES):
                sum_rows(Tile(0, k))
                multiply(Tile(0, k - 1))
            multiply(Tile(0, TILES - 1))


def kernel(x, src, dst, L0_gnn_W, L0_gnn_b):
    import numpy as _np
    import concourse.bacc as _bacc
    from concourse import mybir as _mybir
    from concourse.bass_utils import run_bass_kernel_spmd as _run

    nc = _bacc.Bacc("TRN2", target_bir_lowering=False, num_devices=1)
    given = {"x": x, "edges": _np.stack([src, dst], axis=1), "W": L0_gnn_W, "b": L0_gnn_b}
    arrays, args = {}, []
    for name, a in given.items():
        a = _np.ascontiguousarray(a)
        arrays[f"in_{name}_dram"] = a
        args.append(nc.dram_tensor(f"in_{name}_dram", a.shape, _mybir.dt.from_np(a.dtype), kind="ExternalInput").ap())
    out = nc.dram_tensor("out_0_dram", x.shape, _mybir.dt.from_np(_np.dtype("float32")), kind="ExternalOutput").ap()
    gnn_kernel(nc, *args, out)
    return _run(nc, [arrays], core_ids=[0]).results[0]["out_0_dram"]
```

```python
from contextlib import ExitStack

import concourse.bass as bass
from concourse import mybir

ALU = mybir.AluOpType
ACT = mybir.ActivationFunctionType
AX = mybir.AxisListType
F32 = mybir.dt.float32
F32R = mybir.dt.float32r
BF16 = mybir.dt.bfloat16
F16 = mybir.dt.float16
I32 = mybir.dt.int32

P = 128
EPS = 1e-5
S_LOW, S_FALL, S_STEP, S_SIGNED, S_INVERSE, S_DINV = 4, 8, 16, 17, 19, 25
CONSTS = 11
C_TICKS = 6
UNROLL = 6
HEAD = 7
FAR = 1 << 16


class Tile:

    def __init__(self, i, off):
        self.i, self.off = i, off

    def __add__(self, d):
        return Tile(self.i, self.off + d)

    def __sub__(self, d):
        return Tile(self.i, self.off - d)

    def exists(self, tiles):
        return not isinstance(self.i, int) or 0 <= self.off < tiles

    @property
    def n(self):
        return self.i * UNROLL + self.off

    def slot(self, ring):
        return self.off % ring

    def round(self, ring):
        return self.i * (UNROLL // ring) + self.off // ring


def at_least(eng, sem, value):
    if not isinstance(value, int) or value > 0:
        eng.wait_ge(sem, value)


def gnn_kernel(nc, x, edges, w, b, out):
    NODES, D = x.shape
    EDGES = edges.shape[0]
    KC = D // P
    HALF = D // 2
    TILES = -(-NODES // P)
    LAST_ROWS = NODES - (TILES - 1) * P
    TCOLS = -(-TILES // 8) * 8
    TBLK = TCOLS // 4
    EP = max(p for p in range(1, P + 1) if EDGES % p == 0)
    EC = EDGES // EP
    ROUNDS = (TILES - HEAD - 8) // UNROLL
    LOOP_END = HEAD + ROUNDS * UNROLL
    HIST_UNROLL = 20
    assert D % P == 0 and HALF <= 512 and EC % HIST_UNROLL == 0 and TBLK <= P and TCOLS <= 512

    source_weight = nc.dram_tensor("source_weight", (TCOLS * P, 1), F32, kind="Internal").ap()
    edge_list = nc.dram_tensor("edge_list", (TCOLS * P, 2), I32, kind="Internal").ap()
    node_sums = nc.dram_tensor("node_sums", ((TCOLS + 1) * P, D), F32, kind="Internal").ap()

    with ExitStack() as ctx:
        def sb(name, shape, dt):
            return ctx.enter_context(nc.sbuf_tensor(name, shape, dt))

        def pb(name, shape, dt=F32):
            return ctx.enter_context(nc.psum_tensor(name, shape, dt))

        def sem(name):
            return ctx.enter_context(nc.semaphore(name))

        w_raw = sb("w_raw", [P, KC, D], F32)
        w_hi = sb("w_hi", [P, KC, D], F32R)
        w_lo = sb("w_lo", [P, KC, D], F32R)
        bias = sb("bias", [P, D], F32)
        eps = sb("eps", [P, 1], F32)
        root_of_eps = sb("root_of_eps", [P, 1], F32)
        iota_i = sb("iota_i", [P, TCOLS], I32)
        pid_i = sb("pid_i", [P, 1], I32)
        tile_i = sb("tile_i", [P, TCOLS], I32)
        iota_h = sb("iota_h", [P, TCOLS], F16)
        iota_f = sb("iota_f", [P, P], F32)
        centred = sb("centred", [P, P], F32)
        centre = sb("centre", [P, TCOLS], F32)
        pid_f = sb("pid_f", [P, 1], F32)
        ident = sb("ident", [P, P], F32)
        ones = sb("ones", [P, TCOLS], F32)
        zeros = sb("zeros", [P, D], F32)
        zeros_h = sb("zeros_h", [P, TCOLS], BF16)
        edge_sb = sb("edge_sb", [EP, EC, 2], I32)
        next_edge = sb("next_edge", [EP, 2], I32)
        dst_hi_i = sb("dst_hi_i", [EP, EC], I32)
        dst_lo_i = sb("dst_lo_i", [EP, EC], I32)
        dst_hi = sb("dst_hi", [EP, EC], F32)
        half_less_lo = sb("half_less_lo", [EP, EC], F32)
        hot_hi = sb("hot_hi", [EP, HIST_UNROLL, TCOLS], BF16)
        sign_lo = sb("sign_lo", [EP, HIST_UNROLL, P], BF16)
        falls = sb("falls", [EP, EC], F32)
        fall = sb("fall", [EP, 1], F32)
        degree = sb("degree", [P, TCOLS], F32)
        signed = sb("signed", [P, TCOLS], F32)
        next_pid = sb("next_pid", [P, 1], F32)
        far_pid = sb("far_pid", [P, 1], F32)
        last_row = sb("last_row", [P, 1], F32)
        above = sb("above", [P, P], F32)
        corner = sb("corner", [P, P], F32)
        difference = sb("difference", [P, P], F32)
        inverse = sb("inverse", [P, TCOLS], F32)
        guess = sb("guess", [P, TCOLS], F32)
        newton = sb("newton", [P, TCOLS], F32)
        dinv = sb("dinv", [P, TCOLS], F32)
        dinv_rows = sb("dinv_rows", [TBLK, 4, P], F32)
        tile_edges = sb("tile_edges", [1, TCOLS], F32)
        running = sb("running", [1, TCOLS], F32)
        before = sb("before", [1, TCOLS], F32)
        start_row = sb("start_row", [1, TCOLS], I32)
        most = sb("most", [1, 2], F32)
        general_f = sb("general_f", [1, 1], F32)
        general = sb("general", [1, 1], I32)
        XR, WR, GR, YR, OR = 6, 6, 3, 3, 3
        x_t = sb("x_t", [P, XR, D], F32)
        window = sb("window", [P, WR, 2], I32)
        rel = sb("rel", [P, WR], F32)
        square = sb("square", [P, WR], F32)
        outside = sb("outside", [P, WR], F32)
        index = sb("index", [P, WR], I32)
        g_t = sb("g_t", [P, GR, D], F32)
        g_w = sb("g_w", [P, GR], F32)
        z_t = sb("z_t", [P, 2, D], F32)
        gh_t = sb("gh_t", [P, 2, D], F32R)
        gl_t = sb("gl_t", [P, 2, D], F32R)
        s_t = sb("s_t", [P, 2, P], F32R)
        zh_t = sb("zh_t", [P, 2, KC, P], F32R)
        zl_t = sb("zl_t", [P, 2, KC, P], F32R)
        y_t = sb("y_t", [P, YR, D], F32)
        total = sb("total", [P, YR], F32)
        less_mean = sb("less_mean", [P, YR], F32)
        squares_t = sb("squares_t", [P, 2, D], BF16)
        squares = sb("squares", [P, YR], F32)
        std = sb("std", [P, YR], F32)
        rstd = sb("rstd", [P, YR], F32)
        shift = sb("shift", [P, YR], F32)
        o_t = sb("o_t", [P, OR, D], F32)
        c_src = sb("c_src", [EP, 1], I32)
        c_dst = sb("c_dst", [EP, 1], F32)
        c_to = sb("c_to", [EP, 1], I32)
        c_row = sb("c_row", [EP, 1], F32)
        c_shift = sb("c_shift", [EP, 1], F32)
        c_spare = sb("c_spare", [EP, 1], F32)
        c_weight = sb("c_weight", [EP, 1], F32)
        c_rows_t = sb("c_rows_t", [EP, D], F32)
        c_sum = sb("c_sum", [EP, D], F32)
        c_spread_t = sb("c_spread_t", [EP, P], F32)
        c_same_t = sb("c_same_t", [EP, EP], F32)
        c_earlier = sb("c_earlier", [EP, EP], F32)
        c_below = sb("c_below", [EP, EP], F32)
        own_pair = sb("own_pair", [P, TCOLS, 2], I32)
        sum_ps = pb("sum_ps", [P, 2, 512])
        z_ps = pb("z_ps", [P, 2, 512])
        o_ps = [pb(f"o_ps{k}", [P, 2, 512]) for k in range(2)]
        z_flat = z_ps[:, :, :].rearrange("p a b -> p (a b)")[:, 0:D]

        def halves(row):
            return row.rearrange("p (h n) -> p h n", h=2)

        signed_ps = z_ps[:, 0, 0:TCOLS]
        hist_ps = o_ps[1][:, 0, 0:TCOLS]
        count_ps = z_ps[0:1, 1, 0:TCOLS]
        fall_ps = sum_ps[0:1, 0, 0:1]
        dinv_ps = o_ps[0][0:TBLK, 0, :]

        w_in, b_in, edges_in, next_in = sem("w_in"), sem("b_in"), sem("edges_in"), sem("next_in")
        iotas, consts = sem("iotas"), sem("consts")
        set_up = sem("set_up")
        hot_ready, sign_ready, hot_used = sem("hot_ready"), sem("sign_ready"), sem("hot_used")
        signed_ready, hist_ready = sem("signed_ready"), sem("hist_ready")
        counts_ready, guess_ready = sem("counts_ready"), sem("guess_ready")
        dinv_turned, dinv_copied = sem("dinv_turned"), sem("dinv_copied")
        weights_out, list_out = sem("weights_out"), sem("list_out")
        starts_ready, general_ready = sem("starts_ready"), sem("general_ready")
        w_hi_ready, w_split = sem("w_hi_ready"), sem("w_split")
        ring_zeroed = sem("ring_zeroed")
        x_in = [sem(f"x_in{k}") for k in range(XR)]
        window_in = [sem(f"window_in{k}") for k in range(WR)]
        g_in = [sem(f"g_in{k}") for k in range(GR)]
        o_out = [sem(f"o_out{k}") for k in range(OR)]
        rel_ready, square_ready, outside_ready, index_ready = sem("rel_ready"), sem("square_ready"), sem("outside_ready"), sem("index_ready")
        gh_ready, gl_ready, s_ready, sum_ready = sem("gh_ready"), sem("gl_ready"), sem("s_ready"), sem("sum_ready")
        z_ready, zt_ready, zh_ready, zl_ready = sem("z_ready"), sem("zt_ready"), sem("zh_ready"), sem("zl_ready")
        product_ready, y_ready, yb_ready = sem("product_ready"), sem("y_ready"), sem("yb_ready")
        mean_ready, squares_ready, std_ready = sem("mean_ready"), sem("squares_ready"), sem("std_ready")
        rstd_ready, shift_ready, o_ready = sem("rstd_ready"), sem("shift_ready"), sem("o_ready")
        paced = sem("paced")
        c_rows, c_cur, c_spread, c_turned, c_same = (sem(f"c_{s}") for s in ("rows", "cur", "spread", "turned", "same"))
        c_scaled, c_index, c_summed, c_new, c_out = (sem(f"c_{s}") for s in ("scaled", "index", "summed", "new", "out"))
        c_vec, c_init, own_ready = sem("c_vec"), sem("c_init"), sem("own_ready")
        sums_zeroed, general_done, ones_out = sem("sums_zeroed"), sem("general_done"), sem("ones_out")

        block = ctx.enter_context(nc.Block())

        @block.sync
        def _(sp):
            def load_x(t, rows=P):
                at_least(sp, y_ready, (t - XR).n + 1)
                sp.dma_start(x_t[0:rows, t.slot(XR), :], x[bass.ds(t.n * P, rows), :]
                             ).then_inc(x_in[t.slot(XR)], 16)

            def load_window(t):
                at_least(sp, index_ready, (t - WR).round(3) + 1)
                start = sp.value_load(start_row[0:1, bass.ds(t.n, 1)], min_val=0, max_val=(TCOLS - 1) * P)
                sp.dma_start(window[:, t.slot(WR), :], edge_list[bass.ds(start, P), :]
                             ).then_inc(window_in[t.slot(WR)], 16)

            sp.dma_start(edge_sb[:, :, :], edges.rearrange("(p c) k -> p c k", p=EP)).then_inc(edges_in, 16)
            sp.wait_ge(consts, 1)
            sp.dma_start(next_edge[0:EP - 1, :], edges.rearrange("(p c) k -> p c k", p=EP)[1:EP, 0, :]
                         ).then_inc(next_in, 16)
            sp.dma_start(edge_list[0:EDGES, :], edges).then_inc(list_out, 16)
            sp.dma_start(w_raw[:, :, :], w.rearrange("(c p) n -> p c n", p=P)).then_inc(w_in, 16)
            sp.dma_start(bias[:, :], b.partition_broadcast(P)).then_inc(b_in, 16)
            for k in range(XR):
                load_x(Tile(0, k))
            sp.wait_ge(dinv_copied, 1)
            sp.dma_start(source_weight.rearrange("(k t p) o -> t k (p o)", k=4, p=P), dinv_rows[:, :, :]
                         ).then_inc(weights_out, 16)
            sp.wait_ge(list_out, 16)
            sp.wait_ge(general_ready, 1)
            taken = sp.value_load(general[0:1, 0:1], min_val=0, max_val=1)
            with sp.If(taken > 0):
                with sp.Fori(0, TCOLS + 1) as r:
                    sp.dma_start(node_sums[bass.ds(r * P, P), :], zeros[:, :]).then_inc(sums_zeroed, 16)
                sp.wait_ge(general_done, 1)
            sp.wait_ge(starts_ready, 1)
            for k in range(2 * WR):
                load_window(Tile(0, k))
            with sp.Fori(0, (TILES - 2 * XR) // UNROLL) as i:
                for k in range(XR):
                    load_x(Tile(i, XR + k))
                    load_window(Tile(i, XR + k) + WR)
            done = XR + (TILES - 2 * XR) // UNROLL * UNROLL
            for k in range(done, TILES):
                load_x(Tile(0, k), P if k < TILES - 1 else LAST_ROWS)
                if k + WR < TILES:
                    load_window(Tile(0, k) + WR)

        @block.gpsimd
        def _(pool):
            pool.iota(iota_i[:, :], [[1, TCOLS]], base=0, channel_multiplier=0).then_inc(iotas, 1)
            pool.iota(tile_i[:, :], [[P, TCOLS]], base=0, channel_multiplier=0).then_inc(iotas, 1)
            pool.iota(pid_i[:, :], [[0, 1]], base=0, channel_multiplier=1).then_inc(iotas, 1)
            pool.memset(g_t[:, :, :], 0.0).then_inc(ring_zeroed, 1)
            pool.memset(g_w[:, :], 0.0).then_inc(ring_zeroed, 1)
            pool.wait_ge(ring_zeroed, 2)
            pool.wait_ge(weights_out, 16)
            pool.wait_ge(general_ready, 1)

            def gather(t, rows):
                at_least(pool, index_ready, t.round(3) + 1)
                pool.sem_inc(paced, 1)
                at_least(pool, gl_ready, (t - GR).n + 1)
                pool.sem_inc(paced, 1)
                at = index[:, t.slot(WR):t.slot(WR) + 1]
                pool.indirect_dma_start(out=g_t[:, t.slot(GR), :], out_offset=None, in_=rows,
                                        in_offset=bass.IndirectOffsetOnAxis(ap=at, axis=0),
                                        bounds_check=NODES - 1, oob_is_err=False
                                        ).then_inc(g_in[t.slot(GR)], 16)
                pool.indirect_dma_start(out=g_w[:, t.slot(GR):t.slot(GR) + 1], out_offset=None, in_=source_weight,
                                        in_offset=bass.IndirectOffsetOnAxis(ap=at, axis=0),
                                        bounds_check=NODES - 1, oob_is_err=False
                                        ).then_inc(g_in[t.slot(GR)], 16)

            def gather_all(rows):
                for k in range(HEAD):
                    gather(Tile(0, k), rows)
                with pool.Fori(0, ROUNDS) as i:
                    for k in range(UNROLL):
                        gather(Tile(i, HEAD + k), rows)
                for k in range(LOOP_END, TILES):
                    gather(Tile(0, k), rows)

            def chunk(c):
                pool.wait_ge(c_index, c + 1)
                pool.sem_inc(paced, 1)
                pool.indirect_dma_start(out=c_rows_t[:, :], out_offset=None, in_=x,
                                        in_offset=bass.IndirectOffsetOnAxis(ap=c_src[:, :], axis=0)
                                        ).then_inc(c_rows, 16)
                pool.indirect_dma_start(out=c_weight[:, :], out_offset=None, in_=source_weight,
                                        in_offset=bass.IndirectOffsetOnAxis(ap=c_src[:, :], axis=0)
                                        ).then_inc(c_rows, 16)
                pool.indirect_dma_start(out=c_sum[:, :], out_offset=None, in_=node_sums,
                                        in_offset=bass.IndirectOffsetOnAxis(ap=c_to[:, :], axis=0)
                                        ).then_inc(c_cur, 16)
                pool.wait_ge(c_new, (c + 1) * 2)
                pool.sem_inc(paced, 1)
                pool.indirect_dma_start(out=node_sums, out_offset=bass.IndirectOffsetOnAxis(ap=c_to[:, :], axis=0),
                                        in_=c_sum[:, :], in_offset=None).then_inc(c_out, 16)
                pool.wait_ge(c_out, (c + 1) * 16)

            taken = pool.value_load(general[0:1, 0:1], min_val=0, max_val=1)
            with pool.If(taken > 0):
                pool.wait_ge(sums_zeroed, 16 * (TCOLS + 1))
                with pool.Fori(0, EC) as c:
                    chunk(c)
                pool.iota(own_pair[:, :, :], [[1, TCOLS], [0, 2]], base=0, channel_multiplier=TCOLS
                          ).then_inc(own_ready, 1)
                pool.wait_ge(own_ready, 1)
                pool.dma_start(source_weight.rearrange("(p t) o -> p (t o)", p=P), ones[:, :]).then_inc(ones_out, 16)
                pool.dma_start(edge_list.rearrange("(p t) k -> p (t k)", p=P),
                               own_pair[:, :, :].rearrange("p t k -> p (t k)")).then_inc(ones_out, 16)
                pool.wait_ge(ones_out, 32)
                pool.sem_inc(general_done, 1)
                gather_all(node_sums)
            with pool.Else():
                gather_all(x)

        @block.scalar
        def _(act):
            def sign(c, k):
                nc.scalar.activation(sign_lo[:, k, :], iota_f[0:EP, :], ACT.Sign, bias=half_less_lo[:, bass.ds(c, 1)]
                                     ).then_inc(sign_ready, 1)

            act.wait_ge(consts, CONSTS)
            act.wait_ge(set_up, S_LOW)
            for k in range(HIST_UNROLL):
                sign(k, k)
            with act.Fori(0, EC // HIST_UNROLL - 1) as i:
                for k in range(HIST_UNROLL):
                    act.wait_ge(hot_used, i * HIST_UNROLL + k + 1)
                    sign(i * HIST_UNROLL + HIST_UNROLL + k, k)
            nc.scalar.activation(root_of_eps[:, :], eps[:, :], ACT.Sqrt)
            act.wait_ge(set_up, S_INVERSE)
            nc.scalar.activation(guess[:, :], inverse[:, :], ACT.Sqrt).then_inc(guess_ready, 1)
            act.wait_ge(w_in, 16)
            nc.scalar.copy(w_hi[:, :, :], w_raw[:, :, :]).then_inc(w_hi_ready, 1)

            def gathered_high(t):
                act.wait_ge(g_in[t.slot(GR)], 32 * (t.round(GR) + 1))
                at_least(act, sum_ready, (t - 2).n + 1)
                nc.scalar.activation(gh_t[:, t.slot(2), :], g_t[:, t.slot(GR), :], ACT.Copy,
                                     scale=g_w[:, t.slot(GR):t.slot(GR) + 1]).then_inc(gh_ready, 1)

            def z_high(t):
                act.wait_ge(zt_ready, t.n + 1)
                at_least(act, product_ready, (t - 2).n + 1)
                nc.scalar.copy(zh_t[:, t.slot(2), :, :].rearrange("p c n -> p (c n)"), z_flat).then_inc(zh_ready, 1)

            def spread(t):
                k = t.slot(YR)
                act.wait_ge(mean_ready, t.n + 1)
                nc.scalar.activation(squares_t[:, t.slot(2), :], y_t[:, k, :], ACT.Square, bias=less_mean[:, k:k + 1],
                                     accum_out=squares[:, k:k + 1]).then_inc(squares_ready, 1)
                act.wait_ge(squares_ready, t.n + 1)
                nc.scalar.activation(std[:, k:k + 1], squares[:, k:k + 1], ACT.Sqrt, scale=1.0 / D, bias=eps[:, :]
                                     ).then_inc(std_ready, 1)

            def normalise(t):
                act.wait_ge(shift_ready, t.n + 1)
                at_least(act, o_out[t.slot(OR)], 16 * t.round(OR))
                k = t.slot(YR)
                nc.scalar.activation(o_t[:, t.slot(OR), :], y_t[:, k, :], ACT.Identity, scale=rstd[:, k:k + 1],
                                     bias=shift[:, k:k + 1]).then_inc(o_ready, 1)

            def store(t, rows=P):
                act.wait_ge(o_ready, t.n + 1)
                act.dma_start(out[bass.ds(t.n * P, rows), :], o_t[0:rows, t.slot(OR), :]
                              ).then_inc(o_out[t.slot(OR)], 16)

            def step(t):
                if t.exists(TILES):
                    z_high(t)
                if (t + 2).exists(TILES):
                    gathered_high(t + 2)
                if (t - 4).exists(TILES):
                    normalise(t - 4)
                if (t - 3).exists(TILES):
                    spread(t - 3)
                if (t - 4).exists(TILES):
                    store(t - 4, P if (t - 4).exists(TILES - 1) else LAST_ROWS)

            act.wait_ge(set_up, S_DINV)
            for k in range(2):
                gathered_high(Tile(0, k))
            for k in range(HEAD):
                step(Tile(0, k))
            with act.Fori(0, ROUNDS) as i:
                for k in range(UNROLL):
                    step(Tile(i, HEAD + k))
            for k in range(LOOP_END, TILES + 4):
                step(Tile(0, k))
            for k in range(OR):
                act.wait_ge(o_out[k], 16 * len(range(k, TILES, OR)))

        @block.vector
        def _(dve):
            steps = [0]

            def after(ins):
                ins.then_inc(set_up, 1)
                steps[0] += 1
                return steps[0]

            dve.memset(next_edge[:, :], 1 << 24).then_inc(consts, 1)
            dve.memset(ones[:, :], 1.0).then_inc(consts, 1)
            dve.memset(zeros[:, :], 0.0).then_inc(consts, 1)
            dve.memset(zeros_h[:, :], 0.0).then_inc(consts, 1)
            dve.memset(eps[:, :], EPS).then_inc(consts, 1)
            dve.wait_ge(iotas, 3)
            dve.tensor_copy(iota_h[:, :], iota_i[:, :]).then_inc(consts, 1)
            dve.tensor_copy(iota_f[:, :], iota_i[:, 0:P]).then_inc(consts, 1)
            dve.tensor_scalar(centred[:, :], iota_i[:, 0:P], 63.5, None, ALU.subtract).then_inc(consts, 1)
            dve.tensor_scalar(centre[:, :], tile_i[:, :], 63.5, None, ALU.add).then_inc(consts, 1)
            dve.tensor_copy(pid_f[:, :], pid_i[:, :]).then_inc(consts, 1)
            dve.wait_ge(consts, CONSTS - 1)
            dve.tensor_scalar(ident[:, :], iota_f[:, :], pid_f[:, 0:1], None, ALU.is_equal).then_inc(consts, 1)

            dve.wait_ge(edges_in, 16)
            after(dve.tensor_scalar(dst_hi_i[:, :], edge_sb[:, :, 1], 7, None, ALU.logical_shift_right))
            a = after(dve.tensor_scalar(dst_lo_i[:, :], edge_sb[:, :, 1], P - 1, None, ALU.bitwise_and))
            dve.wait_ge(set_up, a)
            after(dve.tensor_copy(dst_hi[:, :], dst_hi_i[:, :]))
            a = after(dve.tensor_scalar(half_less_lo[:, :], dst_lo_i[:, :], -1.0, 0.5, ALU.mult, ALU.add))
            assert a == S_LOW
            dve.wait_ge(set_up, a)

            def one_hot(c, k):
                dve.tensor_scalar(hot_hi[:, k, :], iota_h[0:EP, :], dst_hi[:, bass.ds(c, 1)], None,
                                  ALU.is_equal).then_inc(hot_ready, 1)

            for k in range(HIST_UNROLL):
                one_hot(k, k)
            with dve.Fori(0, EC // HIST_UNROLL - 1) as i:
                for k in range(HIST_UNROLL):
                    dve.wait_ge(hot_used, i * HIST_UNROLL + k + 1)
                    one_hot(i * HIST_UNROLL + HIST_UNROLL + k, k)

            dve.wait_ge(next_in, 16)
            after(dve.tensor_tensor(falls[:, 0:EC - 1], edge_sb[:, 0:EC - 1, 1], edge_sb[:, 1:EC, 1], ALU.subtract))
            a = after(dve.tensor_tensor(falls[:, EC - 1:EC], edge_sb[:, EC - 1, 1:2], next_edge[:, 1:2], ALU.subtract))
            dve.wait_ge(set_up, a)
            a = after(dve.tensor_reduce(fall[:, :], falls[:, :], AX.X, ALU.max))
            dve.wait_ge(set_up, a)
            a = after(dve.tensor_scalar(fall[:, :], fall[:, :], 0.0, None, ALU.is_gt))
            assert a == S_FALL

            after(dve.tensor_scalar(next_pid[:, :], pid_f[:, :], 1.0, None, ALU.add))
            after(dve.tensor_scalar(far_pid[:, :], pid_f[:, :], float(P - 1), None, ALU.subtract))
            a = after(dve.tensor_scalar(last_row[:, :], pid_f[:, :], float(P - 1), None, ALU.is_equal))
            dve.wait_ge(set_up, a)
            after(dve.tensor_scalar(above[:, :], iota_f[:, :], next_pid[:, 0:1], None, ALU.is_equal))
            a = after(dve.tensor_scalar(corner[:, :], iota_f[:, :], far_pid[:, 0:1], None, ALU.is_equal))
            dve.wait_ge(set_up, a)
            a = after(dve.tensor_tensor(difference[:, :], ident[:, :], above[:, :], ALU.subtract))
            dve.wait_ge(set_up, a)
            a = after(dve.tensor_tensor(difference[:, :], difference[:, :], corner[:, :], ALU.add))
            dve.wait_ge(set_up, a)
            a = after(dve.tensor_scalar(difference[:, :], difference[:, :], 0.5, None, ALU.mult))
            assert a == S_STEP

            dve.wait_ge(signed_ready, 1)
            a = after(dve.tensor_copy(signed[:, :], signed_ps))
            assert a == S_SIGNED
            dve.wait_ge(hist_ready, 1)
            a = after(dve.tensor_scalar(degree[:, :], hist_ps, 1.0, None, ALU.add))
            dve.wait_ge(set_up, a)
            a = after(dve.reciprocal(inverse[:, :], degree[:, :]))
            assert a == S_INVERSE
            dve.wait_ge(counts_ready, 1)
            a = after(dve.tensor_copy(tile_edges[:, :], count_ps))
            dve.wait_ge(set_up, a)
            after(dve.tensor_tensor_scan(running[:, :], tile_edges[:, :], zeros[0:1, 0:TCOLS], 0.0, ALU.add, ALU.add))
            dve.wait_ge(guess_ready, 1)
            a = after(dve.tensor_tensor(newton[:, :], guess[:, :], guess[:, :], ALU.mult))
            dve.wait_ge(set_up, a)
            a = after(dve.tensor_tensor(newton[:, :], newton[:, :], degree[:, :], ALU.mult))
            dve.wait_ge(set_up, a)
            a = after(dve.tensor_scalar(newton[:, :], newton[:, :], -0.5, 1.5, ALU.mult, ALU.add))
            dve.wait_ge(set_up, a)
            a = after(dve.tensor_tensor(dinv[:, :], newton[:, :], guess[:, :], ALU.mult))
            assert a == S_DINV
            after(dve.tensor_tensor(before[:, :], running[:, :], tile_edges[:, :], ALU.subtract))
            a = after(dve.tensor_reduce(most[:, 0:1], tile_edges[:, :], AX.X, ALU.max))
            dve.wait_ge(set_up, a)
            a = after(dve.tensor_scalar(most[:, 1:2], most[:, 0:1], float(P), None, ALU.is_gt))
            dve.wait_ge(set_up, a)
            a = after(dve.tensor_tensor(general_f[:, :], most[:, 1:2], fall_ps, ALU.add))
            dve.wait_ge(set_up, a)
            dve.tensor_scalar(general[:, :], general_f[:, :], 0.0, None, ALU.is_gt).then_inc(general_ready, 1)
            dve.wait_ge(dinv_turned, 1)
            dve.tensor_copy(dinv_rows[:, :, :], dinv_ps.rearrange("t (k p) -> t k p", k=4)).then_inc(dinv_copied, 1)
            dve.wait_ge(general_ready, 1)

            def chunk(c):
                tick = [0]

                def then(ins):
                    ins.then_inc(c_vec, 1)
                    tick[0] += 1
                    dve.wait_ge(c_vec, c * C_TICKS + tick[0])

                dve.tensor_copy(c_src[:, :], edge_sb[:, bass.ds(c, 1), 0]).then_inc(c_vec, 1)
                tick[0] += 1
                then(dve.tensor_copy(c_dst[:, :], edge_sb[:, bass.ds(c, 1), 1]))
                dve.tensor_scalar(c_spread_t[:, :], ones[0:EP, 0:P], c_dst[:, 0:1], None, ALU.mult
                                  ).then_inc(c_spread, 1)
                dve.wait_ge(c_turned, c + 1)
                dve.tensor_scalar(c_same_t[:, :], o_ps[1][0:EP, 0, 0:EP], c_dst[:, 0:1], None, ALU.is_equal
                                  ).then_inc(c_same, 1)
                dve.wait_ge(c_same, c + 1)
                then(dve.tensor_tensor(c_earlier[:, :], c_same_t[:, :], c_below[:, :], ALU.mult))
                then(dve.tensor_reduce(c_spare[:, :], c_earlier[:, :], AX.X, ALU.max))
                then(dve.tensor_tensor(c_shift[:, :], c_row[:, :], c_dst[:, :], ALU.subtract))
                then(dve.tensor_tensor(c_shift[:, :], c_shift[:, :], c_spare[:, :], ALU.mult))
                dve.tensor_tensor(c_to[:, :], c_shift[:, :], c_dst[:, :], ALU.add).then_inc(c_index, 1)
                dve.wait_ge(c_rows, (c + 1) * 32)
                dve.tensor_scalar(c_rows_t[:, :], c_rows_t[:, :], c_weight[:, 0:1], None, ALU.mult
                                  ).then_inc(c_scaled, 1)
                dve.wait_ge(c_summed, c + 1)
                dve.wait_ge(c_cur, (c + 1) * 16)
                for h in range(2):
                    part = c_sum[:, h * HALF:(h + 1) * HALF]
                    dve.tensor_tensor(part, part, o_ps[0][0:EP, h, 0:HALF], ALU.add).then_inc(c_new, 1)
                dve.wait_ge(c_out, (c + 1) * 16)
                assert tick[0] == C_TICKS

            taken = dve.value_load(general[0:1, 0:1], min_val=0, max_val=1)
            with dve.If(taken > 0):
                dve.tensor_scalar(c_below[:, :], iota_f[0:EP, 0:EP], pid_f[0:EP, 0:1], None, ALU.is_lt
                                  ).then_inc(c_init, 1)
                dve.tensor_scalar(c_row[:, :], pid_f[0:EP, :], float(TCOLS * P), None, ALU.add).then_inc(c_init, 1)
                dve.wait_ge(c_init, 2)
                with dve.Fori(0, EC) as c:
                    chunk(c)
                dve.tensor_copy(start_row[:, :], tile_i[0:1, :]).then_inc(starts_ready, 1)
            with dve.Else():
                dve.tensor_scalar(start_row[:, :], before[:, :], float(EDGES - P), None, ALU.min
                                  ).then_inc(starts_ready, 1)

            dve.wait_ge(w_hi_ready, 1)
            dve.tensor_tensor(w_lo[:, :, :], w_raw[:, :, :], w_hi[:, :, :].bitcast(F32), ALU.subtract).then_inc(w_split, 1)

            def make_index(t):
                n = 3 if not isinstance(t.i, int) else min(3, TILES - t.off)
                for k in range(n):
                    u = t + k
                    dve.wait_ge(window_in[u.slot(WR)], 16 * (u.round(WR) + 1))
                a, z = t.slot(WR), t.slot(WR) + n
                done = t.round(3)
                at_least(dve, s_ready, (t - 4).n + 1)
                dve.tensor_tensor(rel[:, a:z], window[:, a:z, 1], centre[:, bass.ds(t.n, n)], ALU.subtract
                                  ).then_inc(rel_ready, 1)
                dve.wait_ge(rel_ready, done + 1)
                dve.tensor_tensor(square[:, a:z], rel[:, a:z], rel[:, a:z], ALU.mult).then_inc(square_ready, 1)
                dve.wait_ge(square_ready, done + 1)
                dve.tensor_scalar(outside[:, a:z], square[:, a:z], 64.0 ** 2, float(FAR), ALU.is_gt, ALU.mult
                                  ).then_inc(outside_ready, 1)
                dve.wait_ge(outside_ready, done + 1)
                dve.tensor_tensor(index[:, a:z], outside[:, a:z], window[:, a:z, 0], ALU.add
                                  ).then_inc(index_ready, 1)

            def gathered_low(t):
                k, g = t.slot(2), t.slot(GR)
                at_least(dve, sum_ready, (t - 2).n + 1)
                dve.wait_ge(gh_ready, t.n + 1)
                dve.scalar_tensor_tensor(out=gl_t[:, k, :], in0=g_t[:, g, :], scalar=g_w[:, g:g + 1],
                                         in1=gh_t[:, k, :].bitcast(F32), op0=ALU.mult, op1=ALU.subtract
                                         ).then_inc(gl_ready, 1)

            def select(t):
                at_least(dve, sum_ready, (t - 2).n + 1)
                dve.tensor_scalar(s_t[:, t.slot(2), :], centred[:, :], rel[:, t.slot(WR):t.slot(WR) + 1], None,
                                  ALU.is_equal).then_inc(s_ready, 1)

            def make_z(t):
                dve.wait_ge(x_in[t.slot(XR)], 16 * (t.round(XR) + 1))
                dve.wait_ge(sum_ready, t.n + 1)
                at_least(dve, zt_ready, (t - 2).n + 1)
                dve.scalar_tensor_tensor(out=halves(z_t[:, t.slot(2), :]), in0=halves(x_t[:, t.slot(XR), :]),
                                         scalar=dinv[:, bass.ds(t.n, 1)], in1=sum_ps[:, :, 0:HALF],
                                         op0=ALU.mult, op1=ALU.add).then_inc(z_ready, 1)

            def z_low(t):
                k = t.slot(2)
                dve.wait_ge(zh_ready, t.n + 1)
                dve.tensor_tensor(zl_t[:, k, :, :].rearrange("p c n -> p (c n)"), z_flat,
                                  zh_t[:, k, :, :].rearrange("p c n -> p (c n)").bitcast(F32), ALU.subtract
                                  ).then_inc(zl_ready, 1)

            def add_up(t):
                k = t.slot(YR)
                dve.wait_ge(product_ready, t.n + 1)
                at_least(dve, o_ready, (t - YR).n + 1)
                dve.scalar_tensor_tensor(out=halves(y_t[:, k, :]), in0=o_ps[t.slot(2)][:, :, 0:HALF],
                                         scalar=dinv[:, bass.ds(t.n, 1)], in1=halves(x_t[:, t.slot(XR), :]),
                                         op0=ALU.mult, op1=ALU.add).then_inc(y_ready, 1)
                dve.wait_ge(y_ready, t.n + 1)
                dve.scalar_tensor_tensor(out=y_t[:, k, :], in0=y_t[:, k, :], scalar=1.0, in1=bias[:, :],
                                         op0=ALU.mult, op1=ALU.add, accum_out=total[:, k:k + 1]
                                         ).then_inc(yb_ready, 1)

            def mean(t):
                k = t.slot(YR)
                dve.wait_ge(yb_ready, t.n + 1)
                dve.tensor_scalar(less_mean[:, k:k + 1], total[:, k:k + 1], -1.0 / D, None, ALU.mult
                                  ).then_inc(mean_ready, 1)

            def finish(t):
                k = t.slot(YR)
                dve.wait_ge(std_ready, t.n + 1)
                dve.reciprocal(rstd[:, k:k + 1], std[:, k:k + 1]).then_inc(rstd_ready, 1)
                dve.wait_ge(rstd_ready, t.n + 1)
                dve.tensor_tensor(shift[:, k:k + 1], less_mean[:, k:k + 1], rstd[:, k:k + 1], ALU.mult
                                  ).then_inc(shift_ready, 1)

            def step(t):
                if (t - 4).exists(TILES):
                    finish(t - 4)
                if t.exists(TILES):
                    z_low(t)
                if (t + 1).exists(TILES):
                    make_z(t + 1)
                if (t - 2).exists(TILES):
                    add_up(t - 2)
                if (t + 2).exists(TILES):
                    gathered_low(t + 2)
                if (t - 2).exists(TILES):
                    mean(t - 2)
                if (t + 2).exists(TILES):
                    select(t + 2)
                if t.off % 3 == 0 and (t + 6).exists(TILES):
                    make_index(t + 6)

            dve.wait_ge(b_in, 16)
            make_index(Tile(0, 0))
            make_index(Tile(0, 3))
            for k in range(2):
                gathered_low(Tile(0, k))
                select(Tile(0, k))
            make_z(Tile(0, 0))
            for k in range(HEAD):
                step(Tile(0, k))
            with dve.Fori(0, ROUNDS) as i:
                for k in range(UNROLL):
                    step(Tile(i, HEAD + k))
            for k in range(LOOP_END, TILES + 4):
                step(Tile(0, k))

        @block.tensor
        def _(pe):
            pe.wait_ge(consts, CONSTS)
            nc.tensor.matmul(signed_ps, zeros_h[:, 0:P], zeros_h[:, :], start=True, stop=False)
            with pe.Fori(0, EC // HIST_UNROLL) as i:
                for k in range(HIST_UNROLL):
                    pe.wait_ge(hot_ready, i * HIST_UNROLL + k + 1)
                    pe.wait_ge(sign_ready, i * HIST_UNROLL + k + 1)
                    nc.tensor.matmul(signed_ps, sign_lo[:, k, :], hot_hi[:, k, :], start=False, stop=False
                                     ).then_inc(hot_used, 1)
            nc.tensor.matmul(signed_ps, zeros_h[:, 0:P], zeros_h[:, :], start=False, stop=True
                             ).then_inc(signed_ready, 1)
            pe.wait_ge(set_up, S_SIGNED)
            nc.tensor.matmul(hist_ps, difference[:, :], signed[:, :], start=True, stop=True).then_inc(hist_ready, 1)
            nc.tensor.matmul(fall_ps, fall[:, :], ones[0:EP, 0:1], start=True, stop=True)
            nc.tensor.matmul(count_ps, last_row[:, :], signed[:, :], start=True, stop=True).then_inc(counts_ready, 1)
            pe.wait_ge(set_up, S_DINV)
            for k in range(4):
                ins = nc.tensor.transpose(dinv_ps[:, k * P:(k + 1) * P], dinv[:, k * TBLK:(k + 1) * TBLK], ident[:, :])
            ins.then_inc(dinv_turned, 1)

            pe.wait_ge(general_ready, 1)
            taken = pe.value_load(general[0:1, 0:1], min_val=0, max_val=1)
            with pe.If(taken > 0):
                pe.wait_ge(dinv_copied, 1)
                with pe.Fori(0, EC) as c:
                    pe.wait_ge(c_spread, c + 1)
                    nc.tensor.transpose(o_ps[1][:, 0, 0:EP], c_spread_t[:, :], ident[0:EP, 0:EP]).then_inc(c_turned, 1)
                    pe.wait_ge(c_scaled, c + 1)
                    for h in range(2):
                        ins = nc.tensor.matmul(o_ps[0][0:EP, h, 0:HALF], c_same_t[:, :],
                                               c_rows_t[:, h * HALF:(h + 1) * HALF], start=True, stop=True)
                    ins.then_inc(c_summed, 1)

            def sum_rows(t):
                k = t.slot(2)
                pe.wait_ge(s_ready, t.n + 1)
                pe.wait_ge(gl_ready, t.n + 1)
                at_least(pe, z_ready, (t - 1).n + 1)
                for part in (gh_t, gl_t):
                    for h in range(2):
                        ins = nc.tensor.matmul(sum_ps[:, h, 0:HALF], s_t[:, k, :], part[:, k, h * HALF:(h + 1) * HALF],
                                               start=(part is gh_t), stop=(part is gl_t))
                ins.then_inc(sum_ready, 1)

            def turn(t):
                pe.wait_ge(z_ready, t.n + 1)
                at_least(pe, zl_ready, (t - 1).n + 1)
                for c in range(KC):
                    ins = nc.tensor.transpose(z_flat[:, c * P:(c + 1) * P], z_t[:, t.slot(2), c * P:(c + 1) * P],
                                              ident[:, :])
                ins.then_inc(zt_ready, 1)

            def multiply(t):
                k = t.slot(2)
                pe.wait_ge(zh_ready, t.n + 1)
                at_least(pe, y_ready, (t - 2).n + 1)
                for c in range(KC):
                    for part in (w_hi, w_lo):
                        for h in range(2):
                            nc.tensor.matmul(o_ps[k][:, h, 0:HALF], zh_t[:, k, c, :],
                                             part[:, c, h * HALF:(h + 1) * HALF],
                                             start=(c == 0 and part is w_hi), stop=False)
                pe.wait_ge(zl_ready, t.n + 1)
                for c in range(KC):
                    for h in range(2):
                        ins = nc.tensor.matmul(o_ps[k][:, h, 0:HALF], zl_t[:, k, c, :],
                                               w_hi[:, c, h * HALF:(h + 1) * HALF], start=False, stop=(c == KC - 1))
                ins.then_inc(product_ready, 1)

            pe.wait_ge(dinv_copied, 1)
            def step(t):
                if t.exists(TILES):
                    turn(t)
                if (t + 1).exists(TILES):
                    sum_rows(t + 1)
                if (t - 1).exists(TILES):
                    multiply(t - 1)

            pe.wait_ge(w_split, 1)
            sum_rows(Tile(0, 0))
            for k in range(HEAD):
                step(Tile(0, k))
            with pe.Fori(0, ROUNDS) as i:
                for k in range(UNROLL):
                    step(Tile(i, HEAD + k))
            for k in range(LOOP_END, TILES + 1):
                step(Tile(0, k))


def kernel(x, src, dst, L0_gnn_W, L0_gnn_b):
    import numpy as _np
    import concourse.bacc as _bacc
    from concourse import mybir as _mybir
    from concourse.bass_utils import run_bass_kernel_spmd as _run

    nc = _bacc.Bacc("TRN2", target_bir_lowering=False, num_devices=1)
    given = {"x": x, "edges": _np.stack([src, dst], axis=1), "W": L0_gnn_W, "b": L0_gnn_b}
    arrays, args = {}, []
    for name, a in given.items():
        a = _np.ascontiguousarray(a)
        arrays[f"in_{name}_dram"] = a
        args.append(nc.dram_tensor(f"in_{name}_dram", a.shape, _mybir.dt.from_np(a.dtype), kind="ExternalInput").ap())
    out = nc.dram_tensor("out_0_dram", x.shape, _mybir.dt.from_np(_np.dtype("float32")), kind="ExternalOutput").ap()
    gnn_kernel(nc, *args, out)
    return _run(nc, [arrays], core_ids=[0]).results[0]["out_0_dram"]
```
